# Optimizing a Trainium2 kernel written in Bass

```python
import numpy as np
import jax
import jax.numpy as jnp

def _softmax(x, axis=-1):
    return jax.nn.softmax(x, axis=axis)

def _gelu(x):
    return jax.nn.gelu(x, approximate=True)

def _silu(x):
    return jax.nn.silu(x)

def _sigmoid(x):
    return jax.nn.sigmoid(x)

def _layernorm(x, axis=-1, eps=1e-05):
    m = jnp.mean(x, axis=axis, keepdims=True)
    v = jnp.var(x, axis=axis, keepdims=True)
    return (x - m) / jnp.sqrt(v + eps)

def _scatter_add(tgt, idx, src, axis=0):
    return tgt.at[idx].add(src)

def _segment_sum(src, seg, n):
    return jax.ops.segment_sum(src, seg, n)
kernel_name = 'mk_cond_resid_d2_seqx_r2_7f5997'

def setup_inputs(seed: int=0):
    np.random.seed(seed)
    _w = jnp.asarray

    def _rec_inputs():
        import jax
        import jax.numpy as jnp
        _rk = jax.random.key(seed)
        x = -0.000125 + 0.9999 * jax.random.normal(jax.random.fold_in(_rk, 1), (8, 512, 512), jnp.float32)
        _lenS = 512 - jax.random.randint(jax.random.fold_in(_rk, 7), (8,), 0, max(1, 512 // 4) + 1, jnp.int32)
        _lenS2 = 512 - jax.random.randint(jax.random.fold_in(_rk, 8), (8,), 0, max(1, 512 // 4) + 1, jnp.int32)
        cond_1024 = 0.00513981 + 1.0024 * jax.random.normal(jax.random.fold_in(_rk, 11), (8, 512), jnp.float32)
        return (x, cond_1024)
    x, cond_1024 = _rec_inputs()

    def _L0_cond_setup():
        import jax, jax.numpy as jnp
        import numpy as np
        IN_FEATURES = 512
        OUT_FEATURES = 512
        BATCH = 32
        SEQ = 512
        EPS = 1e-08
        key = jax.random.key(seed)
        k1, k2, k3 = jax.random.split(key, 3)
        Efou = jax.random.normal(k1, (BATCH, SEQ, IN_FEATURES), dtype=jnp.float32)
        y = jax.random.normal(k2, (BATCH, IN_FEATURES), dtype=jnp.float32)
        weight = jax.random.normal(k3, (IN_FEATURES, OUT_FEATURES), dtype=jnp.float32)
        return {'Efou': Efou, 'y': y, 'weight': weight}
    _L0_cond_all = _L0_cond_setup()
    _L0_cond_in = {k: v for k, v in _L0_cond_all.items() if k in ('weight',)}
    del _L0_cond_all

    def _L1_cond_setup():
        import jax, jax.numpy as jnp
        import numpy as np
        EPS = 1e-08
        key = jax.random.key(seed)
        ks = jax.random.split(key, 8)
        B, S, D, H = (8, 1024, 512, 512)
        scale = 1.0 / np.sqrt(D)
        return {'input_seq': jax.random.normal(ks[0], (B, S, D), dtype=jnp.float32), 'initial_hidden': jax.random.normal(ks[1], (B, H), dtype=jnp.float32), 'W_f': jax.random.normal(ks[2], (H, D), dtype=jnp.float32) * scale, 'b_f': jnp.zeros((H,), dtype=jnp.float32), 'W_i': jax.random.normal(ks[3], (H, D), dtype=jnp.float32) * scale, 'b_i': jnp.zeros((H,), dtype=jnp.float32), 'W_h': jax.random.normal(ks[4], (H, D), dtype=jnp.float32) * scale, 'b_h': jnp.zeros((H,), dtype=jnp.float32)}
    _L1_cond_all = _L1_cond_setup()
    _L1_cond_in = {k: v for k, v in _L1_cond_all.items() if k in ('W_f', 'b_f', 'W_i', 'b_i', 'W_h', 'b_h')}
    del _L1_cond_all
    return {'x': x, 'cond_1024': cond_1024, 'L0_cond_weight': _L0_cond_in['weight'], 'L1_cond_W_f': _L1_cond_in['W_f'], 'L1_cond_b_f': _L1_cond_in['b_f'], 'L1_cond_W_i': _L1_cond_in['W_i'], 'L1_cond_b_i': _L1_cond_in['b_i'], 'L1_cond_W_h': _L1_cond_in['W_h'], 'L1_cond_b_h': _L1_cond_in['b_h']}

def reference(x, cond_1024, L0_cond_weight, L1_cond_W_f, L1_cond_b_f, L1_cond_W_i, L1_cond_b_i, L1_cond_W_h, L1_cond_b_h):
    import jax
    import jax.numpy as jnp

    def _L0_cond_ref(Efou, y, weight):
        import jax, jax.numpy as jnp
        import numpy as np
        IN_FEATURES = 512
        OUT_FEATURES = 512
        BATCH = 32
        SEQ = 512
        EPS = 1e-08
        scale = 1.0 / np.sqrt(np.float32(weight.shape[0]))
        ys = y * scale
        d = jax.lax.rsqrt(jnp.einsum('bi,io->bo', ys * ys, weight * weight) + EPS)
        out = jnp.einsum('bsi,io->bso', Efou * ys[:, None, :], weight) * d[:, None, :]
        return out

    def _L1_cond_ref(input_seq, initial_hidden, W_f, b_f, W_i, b_i, W_h, b_h):
        import jax, jax.numpy as jnp
        import numpy as np
        EPS = 1e-08
        forget_gate = jax.nn.sigmoid(jnp.einsum('bsd,hd->bsh', input_seq, W_f) + b_f)
        input_gate = jax.nn.sigmoid(jnp.einsum('bsd,hd->bsh', input_seq, W_i) + b_i)
        gate_sum = forget_gate + input_gate + EPS
        forget_norm = forget_gate / gate_sum
        input_norm = input_gate / gate_sum
        candidate = jnp.einsum('bsd,hd->bsh', input_seq, W_h) + b_h
        new_info = input_norm * candidate
        log_ret = jnp.log(forget_norm + EPS)
        log_cumprod = jnp.cumsum(log_ret, axis=1)
        B, _, H = log_cumprod.shape
        padded = jnp.concatenate([jnp.zeros((B, 1, H), dtype=log_cumprod.dtype), log_cumprod], axis=1)
        scaling = jnp.exp(log_cumprod[:, -1:, :] - padded[:, :-1, :])
        hidden = jnp.cumsum(scaling * new_info, axis=1)
        hidden = hidden + jnp.exp(log_cumprod) * initial_hidden[:, None, :]
        return hidden
    x = x + _L0_cond_ref(x, cond_1024, L0_cond_weight)
    x = x + _L1_cond_ref(x, cond_1024, L1_cond_W_f, L1_cond_b_f, L1_cond_W_i, L1_cond_b_i, L1_cond_W_h, L1_cond_b_h)
    return x

_drawn_inputs = setup_inputs


def setup_inputs(seed=0):
    import zlib

    import numpy as np

    out = dict(_drawn_inputs(seed))
    spreads = {'L1_cond_b_f': (0.0, 0.8), 'L1_cond_b_i': (0.0, 0.8), 'L1_cond_b_h': (0.0, 0.8)}
    factors = {'L1_cond_W_f': 6.228, 'L1_cond_W_i': 7.557, 'L1_cond_W_h': 4.47}
    for name, (base, spread) in spreads.items():
        noise = np.random.default_rng([zlib.crc32(name.encode()), seed]).standard_normal(out[name].shape)
        drawn = base * np.exp(spread * noise) if base else spread * noise
        out[name] = jnp.asarray(drawn.astype(out[name].dtype))
    for name, factor in factors.items():
        out[name] = (out[name] * factor).astype(out[name].dtype)
    return out
```

```python
from contextlib import ExitStack

import numpy as np

import concourse.bass as bass
from concourse import mybir

F32 = mybir.dt.float32
F32R = mybir.dt.float32r
ALU = mybir.AluOpType
ACT = mybir.ActivationFunctionType

P = 128
B, S, D = 8, 512, 512
KT = D // P
TU = 2
UNITS = B * KT // TU
GATES = 3
LAYER_EPS = 1e-8
GATE_EPS = 1e-8
Y_SCALE = float(np.float32(1.0) / np.sqrt(np.float32(D)))
LN_EXP_SET = "natural_log_exp_and_others"


def build(nc, x_d, y_d, bias_d, w_d, out_d):
    with ExitStack() as ctx:
        def sbuf(name, shape, dt=F32):
            return ctx.enter_context(nc.sbuf_tensor(name, shape, dt))

        def bank(name):
            return ctx.enter_context(nc.psum_tensor(name, [P, S], F32))

        def sem(name):
            return ctx.enter_context(nc.semaphore(name))

        w_hi = [sbuf(f"w_hi{m}", [P, KT, D], F32R) for m in range(1 + GATES)]
        w_lo = [sbuf(f"w_lo{m}", [P, KT, D], F32R) for m in range(1 + GATES)]
        y = sbuf("y", [P, KT, B])
        bias = sbuf("bias", [P, GATES, KT])
        ys = sbuf("ys", [P, KT, B])
        ys_sq = sbuf("ys_sq", [P, KT, B])
        demod_sum = sbuf("demod_sum", [P, KT, B])
        demod_root = sbuf("demod_root", [P, KT, B])
        demod_seed = sbuf("demod_seed", [P, KT, B])
        demod = sbuf("demod", [P, KT, B])
        x_in = [sbuf(f"x_in{p}", [P, KT, S]) for p in range(2)]
        xs_hi = [sbuf(f"xs_hi{p}", [P, KT, S], F32R) for p in range(2)]
        xs_lo = [sbuf(f"xs_lo{p}", [P, KT, S], F32R) for p in range(2)]
        x1 = [sbuf(f"x1_{p}", [P, KT, S]) for p in range(2)]
        x1_hi = [sbuf(f"x1_hi{p}", [P, KT, S], F32R) for p in range(2)]
        x1_lo = [sbuf(f"x1_lo{p}", [P, KT, S], F32R) for p in range(2)]
        work = sbuf("work", [P, 2, 5, TU, S])
        forget = [work[:, p, 0] for p in range(2)]
        value = [work[:, p, 1] for p in range(2)]
        gsum = [work[:, p, 2] for p in range(2)]
        seed = [work[:, p, 3] for p in range(2)]
        ret = [work[:, p, 4] for p in range(2)]
        stage = [x1[0][:], work[:, 0, 0:4].rearrange("p a t s -> p (a t) s")[:, 0:4],
                 work[:, 0, 0:4].rearrange("p a t s -> p (a t) s")[:, 4:8],
                 work[:, 1, 0:4].rearrange("p a t s -> p (a t) s")[:, 0:4]]
        w0_sq = x1[1]

        layer0_ps = [bank(f"layer0_ps{i}") for i in range(2)]
        gate_ps = [[bank(f"gate_ps{g}_{i}") for i in range(2)] for g in range(GATES)]
        demod_ps = layer0_ps[1]

        y_loaded = sem("y_loaded")
        bias_loaded = sem("bias_loaded")
        w_loaded = [sem(f"w_loaded{m}") for m in range(1 + GATES)]
        x_loaded = [sem(f"x_loaded{p}") for p in range(2)]
        out_stored = [sem(f"out_stored{p}") for p in range(2)]
        ys_done = sem("ys_done")
        w0_sq_done = sem("w0_sq_done")
        demod_mm = sem("demod_mm")
        demod_step = sem("demod_step")
        root_done = sem("root_done")
        w_hi_done = sem("w_hi_done")
        w_lo_done = sem("w_lo_done")
        xs_hi_done = sem("xs_hi_done")
        xs_lo_done = sem("xs_lo_done")
        layer0_mm = sem("layer0_mm")
        x1_done = sem("x1_done")
        x1_hi_done = sem("x1_hi_done")
        x1_lo_done = sem("x1_lo_done")
        gate_mm = [sem(f"gate_mm{g}") for g in range(GATES)]
        sig_f_done = sem("sig_f_done")
        sig_i_done = sem("sig_i_done")
        gsum_done = sem("gsum_done")
        cand_done = sem("cand_done")
        ln_done = sem("ln_done")
        seed_done = sem("seed_done")
        newton_done = sem("newton_done")
        recip_done = sem("recip_done")
        fnorm_done = sem("fnorm_done")
        info_done = sem("info_done")
        ret_done = sem("ret_done")
        suffix_done = sem("suffix_done")
        scaled_done = sem("scaled_done")
        prefix_done = sem("prefix_done")
        cumsum_done = sem("cumsum_done")
        hidden_done = sem("hidden_done")
        out_done = sem("out_done")

        UNIT_ORDER = [[("gates", 0), ("layer0", 0), ("gates", 1), ("layer0", 1)],
                      [("gates", 2), ("layer0", 2), ("layer0", 3), ("gates", 3)]]

        block = ctx.enter_context(nc.Block())

        @block.sync
        def _(sp):
            def load_x(b, q):
                sp.dma_start(x_in[q][:], x_d[b]).then_inc(x_loaded[q], 16)

            def reload_x(b, q):
                sp.wait_ge(x1_done, KT * (b - 2) + KT)
                load_x(b, q)

            def store(u, b, q, h):
                sp.wait_ge(out_done, u + 1)
                sp.dma_start(out_d[b, :, TU * h:TU * h + TU, :],
                             x1[q][:, TU * h:TU * h + TU, :]).then_inc(out_stored[h], 16)

            sp.dma_start(y[:], y_d).then_inc(y_loaded, 16)
            sp.dma_start(stage[0], w_d[0]).then_inc(w_loaded[0], 16)
            load_x(0, 0)
            for m in (1, 2, 3):
                sp.dma_start(stage[m], w_d[m]).then_inc(w_loaded[m], 16)
            sp.dma_start(bias[:], bias_d).then_inc(bias_loaded, 16)
            load_x(1, 1)
            reload_x(2, 0)
            with sp.Fori(0, 2) as j:
                for q in range(2):
                    for h in range(2):
                        store(4 * j + 2 * q + h, 2 * j + q, q, h)
                    reload_x(2 * j + 3 + q, 1 - q)
            for b in range(4, B):
                for h in range(2):
                    store(2 * b + h, b, b % 2, h)
                if b == 4:
                    reload_x(7, 1)
            for h in range(2):
                sp.wait_ge(out_stored[h], 16 * B)

        @block.tensor
        def _(pe):
            def split_product(ps, m, ht, x_hi, x_lo, ready, base):
                cols = slice(ht * P, ht * P + P)
                for kt in range(KT):
                    if ready is not None:
                        pe.wait_ge(ready, base + kt + 1)
                    pe.matmul(ps[:], w_hi[m][:, kt, cols], x_hi[:, kt, :], start=kt == 0, stop=False)
                    pe.matmul(ps[:], w_lo[m][:, kt, cols], x_hi[:, kt, :], start=False, stop=False)
                    last = pe.matmul(ps[:], w_hi[m][:, kt, cols], x_lo[:, kt, :], start=False,
                                     stop=kt == KT - 1)
                return last

            def layer0(b, q, ht, first):
                n = KT * b + ht
                if not first or ht >= 2:
                    pe.wait_ge(x1_done, n - 1)
                split_product(layer0_ps[ht % 2], 0, ht, xs_hi[q], xs_lo[q],
                              xs_lo_done if ht == 0 else None, KT * b).then_inc(layer0_mm, 1)

            def gates(b, q, ht, first):
                n = KT * b + ht
                for g in range(GATES):
                    if first and ht == 0:
                        pe.wait_ge(w_lo_done, 2 + g)
                    if not first or ht >= 2:
                        pe.wait_ge((sig_f_done, sig_i_done, cand_done)[g], n - 1)
                    split_product(gate_ps[g][ht % 2], 1 + g, ht, x1_hi[q], x1_lo[q],
                                  x1_lo_done if ht == 0 and g == 0 else None, KT * b)\
                        .then_inc(gate_mm[g], 1)

            def phase(b, q, first=False, last=False):
                for h in range(2):
                    for what, ht in UNIT_ORDER[h]:
                        if what == "gates":
                            gates(b, q, ht, first)
                        elif not last:
                            layer0(b + 1, 1 - q, ht, False)

            pe.wait_ge(ys_done, 2)
            pe.wait_ge(w0_sq_done, 1)
            for ht in range(KT):
                for kt in range(KT):
                    last = pe.matmul(demod_ps[:, ht * B:ht * B + B], w0_sq[:, kt, ht * P:ht * P + P],
                                     ys_sq[:, kt, :], start=kt == 0, stop=kt == KT - 1)
            last.then_inc(demod_mm, 1)
            pe.wait_ge(w_lo_done, 1)
            for ht in range(KT):
                if ht == 1:
                    pe.wait_ge(demod_step, 1)
                layer0(0, 0, ht, True)
            phase(0, 0, first=True)
            with pe.Fori(0, 3) as j:
                phase(2 * j + 1, 1)
                phase(2 * j + 2, 0)
            phase(B - 1, 1, last=True)

        @block.scalar
        def _(act):
            def split_x(b, q):
                for kt in range(KT):
                    act.activation(xs_hi[q][:, kt, :], x_in[q][:, kt, :], ACT.Copy,
                                   scale=ys[:, kt, bass.ds(b, 1)]).then_inc(xs_hi_done, 1)

            def split_x1(b, q, ht):
                act.wait_ge(x1_done, KT * b + ht + 1)
                act.activation(x1_hi[q][:, ht, :], x1[q][:, ht, :], ACT.Copy).then_inc(x1_hi_done, 1)

            def split_w(m):
                act.wait_ge(w_loaded[m], 16)
                act.activation(w_hi[m][:], stage[m], ACT.Copy).then_inc(w_hi_done, 1)

            def sigmoids(b, ht, v):
                n = KT * b + ht
                for g, (dst, done) in enumerate(((forget[v], sig_f_done), (value[v], sig_i_done))):
                    act.wait_ge(gate_mm[g], n + 1)
                    act.activation(dst[:, ht % TU, :], gate_ps[g][ht % 2][:], ACT.Sigmoid,
                                   bias=bias[:, g, ht:ht + 1]).then_inc(done, 1)

            def recip_seed(u, v):
                act.preload_act_table_set(LN_EXP_SET)
                act.wait_ge(gsum_done, TU * u + TU)
                act.activation(seed[v], gsum[v], ACT.Ln).then_inc(ln_done, 1)
                act.wait_ge(ln_done, u + 1)
                act.activation(seed[v], seed[v], ACT.Exp, scale=-1.0).then_inc(seed_done, 1)

            def retention(u, v):
                act.wait_ge(fnorm_done, u + 1)
                act.activation(ret[v], forget[v], ACT.Copy, bias=GATE_EPS, scale=-1.0)\
                    .then_inc(ret_done, 1)

            def step(u, b, q, h, load_next, split=None, has_front=True, has_layer0=True, free=True):
                v = (2 * q + h + 1) % 2
                if split is not None:
                    sb, sq, index = split
                    act.wait_ge(x_loaded[sq], 16 * (index + 1))
                    act.wait_ge(layer0_mm, KT * (sb - 2) + KT)
                    split_x(sb, sq)
                recip_seed(u, v)
                if not has_front:
                    retention(u, v)
                    return
                if free:
                    act.wait_ge(out_done, u)
                for k, (what, ht) in enumerate(UNIT_ORDER[h]):
                    if what == "gates":
                        sigmoids(b, ht, 1 - v)
                    elif has_layer0:
                        split_x1(b + 1, 1 - q, ht)
                    if k == 0:
                        retention(u, v)

            act.wait_ge(w_loaded[0], 16)
            act.activation(w0_sq[:], stage[0], ACT.Square).then_inc(w0_sq_done, 1)
            split_w(0)
            act.wait_ge(ys_done, 1)
            act.wait_ge(x_loaded[0], 16)
            split_x(0, 0)
            act.wait_ge(demod_step, 1)
            act.activation(demod_root[:], demod_sum[:], ACT.Sqrt).then_inc(root_done, 1)
            split_w(1)
            split_x1(0, 0, 0)
            split_x1(0, 0, 1)
            split_w(2)
            split_x1(0, 0, 2)
            split_x1(0, 0, 3)
            split_w(3)
            act.wait_ge(x_loaded[1], 16)
            split_x(1, 1)
            act.wait_ge(bias_loaded, 16)
            for what, ht in UNIT_ORDER[0]:
                if what == "gates":
                    sigmoids(0, ht, 0)
                else:
                    split_x1(1, 1, ht)
            step(0, 0, 0, 1, False, free=False)
            with act.Fori(0, 3) as j:
                for k in range(1, 5):
                    u = 4 * j + k
                    front = k + 1
                    split = (2 * j + (k - 1) // 2 + 2, (k - 1) // 2 % 2, j + 1) if k % 2 else None
                    step(u, 2 * j + front // 2, front // 2 % 2, front % 2, False, split)
            step(13, 7, 1, 0, False, has_layer0=False)
            step(14, 7, 1, 1, False, has_layer0=False)
            step(15, None, 1, 0, False, has_front=False)

        @block.vector
        def _(dve):
            def split_x(b, q):
                for kt in range(KT):
                    dve.wait_ge(xs_hi_done, KT * b + kt + 1)
                    dve.scalar_tensor_tensor(xs_lo[q][:, kt, :], x_in[q][:, kt, :],
                                             ys[:, kt, bass.ds(b, 1)], xs_hi[q][:, kt, :].bitcast(F32),
                                             ALU.mult, ALU.subtract).then_inc(xs_lo_done, 1)

            def split_w(m):
                dve.wait_ge(w_hi_done, m + 1)
                dve.tensor_tensor(w_lo[m][:], stage[m], w_hi[m][:].bitcast(F32), ALU.subtract)\
                    .then_inc(w_lo_done, 1)

            def residual0(b, q, ht):
                dve.wait_ge(layer0_mm, KT * b + ht + 1)
                dve.scalar_tensor_tensor(x1[q][:, ht, :], layer0_ps[ht % 2][:],
                                         demod[:, ht, bass.ds(b, 1)], x_in[q][:, ht, :],
                                         ALU.mult, ALU.add).then_inc(x1_done, 1)

            def split_x1(b, q, ht):
                dve.wait_ge(x1_hi_done, KT * b + ht + 1)
                dve.tensor_tensor(x1_lo[q][:, ht, :], x1[q][:, ht, :], x1_hi[q][:, ht, :].bitcast(F32),
                                  ALU.subtract).then_inc(x1_lo_done, 1)

            def gate_sum(b, ht, v):
                t = ht % TU
                dve.wait_ge(sig_i_done, KT * b + ht + 1)
                dve.scalar_tensor_tensor(gsum[v][:, t, :], forget[v][:, t, :], GATE_EPS,
                                         value[v][:, t, :], ALU.add, ALU.add).then_inc(gsum_done, 1)

            def candidate(b, ht, v):
                t = ht % TU
                dve.wait_ge(gate_mm[2], KT * b + ht + 1)
                dve.wait_ge(gsum_done, KT * b + ht + 1)
                dve.scalar_tensor_tensor(value[v][:, t, :], gate_ps[2][ht % 2][:],
                                         bias[:, 2, ht:ht + 1], value[v][:, t, :],
                                         ALU.add, ALU.mult).then_inc(cand_done, 1)

            def norms(u, v):
                dve.wait_ge(seed_done, u + 1)
                dve.tensor_tensor(gsum[v], gsum[v], seed[v], ALU.mult).then_inc(newton_done, 1)
                dve.wait_ge(newton_done, u + 1)
                dve.scalar_tensor_tensor(gsum[v], gsum[v], 2.0, seed[v], ALU.subtract, ALU.mult)\
                    .then_inc(recip_done, 1)
                dve.wait_ge(recip_done, u + 1)
                dve.tensor_tensor(forget[v], forget[v], gsum[v], ALU.mult).then_inc(fnorm_done, 1)
                dve.wait_ge(cand_done, TU * u + TU)
                dve.tensor_tensor(value[v], value[v], gsum[v], ALU.mult).then_inc(info_done, 1)

            def suffix_products(u, v):
                dve.wait_ge(ret_done, u + 1)
                for t in range(TU):
                    dve.tensor_tensor_scan(forget[v][:, t, ::-1], ret[v][:, t, ::-1],
                                           ret[v][:, t, ::-1], 1.0, ALU.mult, ALU.bypass)\
                        .then_inc(suffix_done, 1)

            def scaled_info(u, v):
                dve.wait_ge(info_done, u + 1)
                dve.wait_ge(suffix_done, TU * u + TU)
                dve.tensor_tensor(value[v], value[v], forget[v], ALU.mult).then_inc(scaled_done, 1)

            def prefix_products(u, v, b, h):
                for t in range(TU):
                    dve.tensor_tensor_scan(ret[v][:, t, :], ret[v][:, t, :], ret[v][:, t, :],
                                           y[:, TU * h + t, bass.ds(b, 1)], ALU.mult, ALU.bypass)\
                        .then_inc(prefix_done, 1)

            def cumsums(u, v):
                dve.wait_ge(scaled_done, u + 1)
                for t in range(TU):
                    dve.tensor_tensor_scan(value[v][:, t, :], value[v][:, t, :], value[v][:, t, :], 0.0,
                                           ALU.add, ALU.bypass).then_inc(cumsum_done, 1)

            def hidden(u, v):
                dve.wait_ge(prefix_done, TU * u + TU)
                dve.wait_ge(cumsum_done, TU * u + TU)
                dve.tensor_tensor(ret[v], ret[v], value[v], ALU.subtract).then_inc(hidden_done, 1)

            def output(u, v, q, h):
                dve.wait_ge(hidden_done, u + 1)
                part = x1[q][:, TU * h:TU * h + TU, :]
                dve.tensor_tensor(part, part, ret[v], ALU.add).then_inc(out_done, 1)

            def step(u, b, q, h, bu, split=None, stored=None, has_layer0=True):
                v = (h + 1) % 2
                w = 1 - v
                hu = v
                qu = q if h else 1 - q
                if split is not None:
                    split_x(*split)
                norms(u, v)
                front = UNIT_ORDER[h]

                def take(k):
                    what, ht = front[k]
                    if what == "gates":
                        gate_sum(b, ht, w)
                        candidate(b, ht, w)
                    elif has_layer0:
                        if k == 1 and stored is not None:
                            dve.wait_ge(out_stored[v ^ 1], 16 * stored)
                        residual0(b + 1, 1 - q, ht)
                        if k == 1:
                            return ht
                        split_x1(b + 1, 1 - q, ht)
                    return None

                take(0)
                suffix_products(u, v)
                take(1)
                scaled_info(u, v)
                if has_layer0:
                    split_x1(b + 1, 1 - q, front[1][1])
                prefix_products(u, v, bu, hu)
                cumsums(u, v)
                if front[2][0] == "layer0":
                    take(2)
                    hidden(u, v)
                    output(u, v, qu, hu)
                else:
                    hidden(u, v)
                    output(u, v, qu, hu)
                    take(2)
                take(3)

            dve.wait_ge(y_loaded, 16)
            dve.tensor_scalar(ys[:], y[:], Y_SCALE, None, ALU.mult).then_inc(ys_done, 1)
            dve.wait_ge(ys_done, 1)
            dve.tensor_tensor(ys_sq[:], ys[:], ys[:], ALU.mult).then_inc(ys_done, 1)
            split_w(0)
            split_x(0, 0)
            flat = [t[:].rearrange("p k b -> p (k b)")
                    for t in (demod_sum, demod_root, demod_seed, demod)]
            total, root, first, d = flat
            dve.wait_ge(demod_mm, 1)
            dve.tensor_scalar(total, demod_ps[:, 0:KT * B], LAYER_EPS, None, ALU.add)\
                .then_inc(demod_step, 1)
            dve.wait_ge(root_done, 1)
            dve.reciprocal(first, root).then_inc(demod_step, 1)
            dve.wait_ge(demod_step, 2)
            dve.tensor_tensor(d, total, first, ALU.mult).then_inc(demod_step, 1)
            dve.wait_ge(demod_step, 3)
            dve.tensor_tensor(d, d, first, ALU.mult).then_inc(demod_step, 1)
            dve.wait_ge(demod_step, 4)
            dve.tensor_scalar(d, d, -0.5, 1.5, ALU.mult, ALU.add).then_inc(demod_step, 1)
            dve.wait_ge(demod_step, 5)
            dve.tensor_tensor(d, d, first, ALU.mult).then_inc(demod_step, 1)
            dve.wait_ge(demod_step, 6)
            residual0(0, 0, 0)
            residual0(0, 0, 1)
            split_w(1)
            split_x1(0, 0, 0)
            residual0(0, 0, 2)
            split_x1(0, 0, 1)
            residual0(0, 0, 3)
            split_w(2)
            split_x1(0, 0, 2)
            split_x1(0, 0, 3)
            split_w(3)
            split_x(1, 1)
            dve.wait_ge(bias_loaded, 16)
            for what, ht in UNIT_ORDER[0]:
                if what == "gates":
                    gate_sum(0, ht, 0)
                    candidate(0, ht, 0)
                else:
                    residual0(1, 1, ht)
                    split_x1(1, 1, ht)
            step(0, 0, 0, 1, 0)
            with dve.Fori(0, 3) as j:
                for k in range(1, 5):
                    front = k + 1
                    split = (2 * j + (k - 1) // 2 + 2, (k - 1) // 2 % 2) if k % 2 else None
                    step(4 * j + k, 2 * j + front // 2, front // 2 % 2, front % 2, 2 * j + k // 2,
                         split, 2 * j + (k - 1) // 2 + 1)
            step(13, 7, 1, 0, 6, has_layer0=False)
            step(14, 7, 1, 1, 7, has_layer0=False)
            norms(15, 1)
            suffix_products(15, 1)
            scaled_info(15, 1)
            prefix_products(15, 1, 7, 1)
            cumsums(15, 1)
            hidden(15, 1)
            output(15, 1, 1, 1)


def kernel(x, cond_1024, L0_cond_weight, L1_cond_W_f, L1_cond_b_f, L1_cond_W_i, L1_cond_b_i,
           L1_cond_W_h, L1_cond_b_h):
    import concourse.bacc as bacc
    from concourse.bass_utils import run_bass_kernel_spmd

    def tiled(a):
        return np.asarray(a).reshape(KT, P, -1).transpose(1, 0, 2)

    arrays = {
        "x": np.ascontiguousarray(np.asarray(x).reshape(B, S, KT, P).transpose(0, 3, 2, 1)),
        "y": np.ascontiguousarray(tiled(np.asarray(cond_1024).T)),
        "bias": np.ascontiguousarray(np.stack(
            [np.asarray(v).reshape(KT, P).T for v in (L1_cond_b_f, L1_cond_b_i, L1_cond_b_h)], axis=1)),
        "w": np.ascontiguousarray(np.stack(
            [tiled(L0_cond_weight)] + [tiled(np.asarray(w).T) for w in (L1_cond_W_f, L1_cond_W_i, L1_cond_W_h)])),
    }
    nc = bacc.Bacc("TRN2", target_bir_lowering=False, num_devices=1)
    aps = {n: nc.dram_tensor("in_" + n, a.shape, F32, kind="ExternalInput").ap() for n, a in arrays.items()}
    out = nc.dram_tensor("out", (B, P, KT, S), F32, kind="ExternalOutput").ap()
    build(nc, aps["x"], aps["y"], aps["bias"], aps["w"], out)
    r = run_bass_kernel_spmd(nc, [{"in_" + n: a for n, a in arrays.items()}], core_ids=[0])
    return np.ascontiguousarray(r.results[0]["out"].transpose(0, 3, 2, 1)).reshape(B, S, D)
```

```python
from contextlib import ExitStack

import numpy as np

import concourse.bass as bass
from concourse import mybir

F32 = mybir.dt.float32
F32R = mybir.dt.float32r
BF16 = mybir.dt.bfloat16
ALU = mybir.AluOpType
ACT = mybir.ActivationFunctionType

P = 128
B, S, D = 8, 512, 512
KT = D // P
TU = 2
UNITS = B * KT // TU
WARM = 10
GATES = 3
LAYER_EPS = 1e-8
GATE_EPS = 1e-8
Y_SCALE = float(np.float32(1.0) / np.sqrt(np.float32(D)))
LN_EXP_SET = "natural_log_exp_and_others"
SIGMOID_SET = "sigmoid_and_others"


def build(nc, x_d, y_d, bias_d, w_d, out_d):
    with ExitStack() as ctx:
        def sbuf(name, shape, dt=F32):
            return ctx.enter_context(nc.sbuf_tensor(name, shape, dt))

        def bank(name):
            return ctx.enter_context(nc.psum_tensor(name, [P, S], F32))

        def sem(name):
            return ctx.enter_context(nc.semaphore(name))

        w_hi = [sbuf(f"w_hi{m}", [P, KT, D], F32R) for m in range(1 + GATES)]
        w_lo = [sbuf(f"w_lo{m}", [P, KT, D], F32R) for m in range(1 + GATES)]
        y = sbuf("y", [P, KT, B])
        bias = sbuf("bias", [P, GATES, KT])
        ys = sbuf("ys", [P, KT, B])
        ys_sq = sbuf("ys_sq", [P, KT, B])
        ys_sq_parts = sbuf("ys_sq_parts", [P, KT, 2, B], F32R)
        demod_sum = sbuf("demod_sum", [P, KT, B])
        demod_root = sbuf("demod_root", [P, KT, B])
        demod_seed = sbuf("demod_seed", [P, KT, B])
        demod = sbuf("demod", [P, KT, B])
        x_in = [sbuf(f"x_in{p}", [P, KT, S]) for p in range(2)]
        xs_hi = [sbuf(f"xs_hi{p}", [P, KT, S], F32R) for p in range(2)]
        xs_lo = [sbuf(f"xs_lo{p}", [P, KT, S], F32R) for p in range(2)]
        x1 = [sbuf(f"x1_{p}", [P, KT, S]) for p in range(2)]
        x1_hi = [sbuf(f"x1_hi{p}", [P, KT, S], F32R) for p in range(2)]
        x1_lo = [sbuf(f"x1_lo{p}", [P, KT, S], F32R) for p in range(2)]
        work = sbuf("work", [P, 2, 5, TU, S])
        forget = [work[:, p, 0] for p in range(2)]
        value = [work[:, p, 1] for p in range(2)]
        gsum = [work[:, p, 2] for p in range(2)]
        seed = [work[:, p, 3] for p in range(2)]
        ret = [work[:, p, 4] for p in range(2)]
        even, odd = (work[:, p, 0:4].rearrange("p a t s -> p (a t) s") for p in range(2))
        stage = [x1[0][:], even[:, 0:KT], even[:, KT:2 * KT], odd[:, 0:KT]]
        w0_sq, w0_sq_hi, w0_sq_lo = x1[1], x1_hi[1], x1_lo[1]

        warm = sbuf("warm", [P, S], BF16)

        layer0_ps = [bank(f"layer0_ps{i}") for i in range(2)]
        gate_ps = [[bank(f"gate_ps{g}_{i}") for i in range(2)] for g in range(GATES)]
        demod_ps = gate_ps[2][0]
        early_ps = {(0, 0): layer0_ps[0], (0, 1): layer0_ps[1], (0, 2): gate_ps[1][0],
                    (0, 3): gate_ps[2][1], (1, 0): gate_ps[0][1], (1, 1): gate_ps[1][1]}
        late_cand_ps = [gate_ps[2][0], gate_ps[2][1], layer0_ps[0], layer0_ps[1]]

        y_loaded = sem("y_loaded")
        bias_loaded = sem("bias_loaded")
        w0_loaded = [sem(f"w0_loaded{kt}") for kt in range(KT)]
        w_loaded = {m: sem(f"w_loaded{m}") for m in range(1, 1 + GATES)}
        x0_loaded = [sem(f"x0_loaded{kt}") for kt in range(KT)]
        x_loaded = [sem(f"x_loaded{p}") for p in range(2)]
        out_stored = [sem(f"out_stored{p}") for p in range(2)]
        ys_done = sem("ys_done")
        w0_hi_done = sem("w0_hi_done")
        w0_lo_done = sem("w0_lo_done")
        w0_sq_done = sem("w0_sq_done")
        w0_sq_lo_done = sem("w0_sq_lo_done")
        demod_mm = sem("demod_mm")
        demod_step = sem("demod_step")
        root_done = sem("root_done")
        w_hi_done = sem("w_hi_done")
        w_lo_done = sem("w_lo_done")
        xs_hi_done = sem("xs_hi_done")
        xs_lo_done = sem("xs_lo_done")
        layer0_mm = sem("layer0_mm")
        x1_done = sem("x1_done")
        x1_hi_done = sem("x1_hi_done")
        x1_lo_done = sem("x1_lo_done")
        gate_mm = [sem(f"gate_mm{g}") for g in range(GATES)]
        sig_f_done = sem("sig_f_done")
        sig_i_done = sem("sig_i_done")
        gsum_done = sem("gsum_done")
        cand_done = sem("cand_done")
        ln_done = sem("ln_done")
        seed_done = sem("seed_done")
        newton_done = sem("newton_done")
        recip_done = sem("recip_done")
        fnorm_done = sem("fnorm_done")
        info_done = sem("info_done")
        ret_done = sem("ret_done")
        suffix_done = sem("suffix_done")
        scaled_done = sem("scaled_done")
        prefix_done = sem("prefix_done")
        cumsum_done = sem("cumsum_done")
        prefix_added = sem("prefix_added")
        cumsum_added = sem("cumsum_added")
        last_seed = sem("last_seed")
        last_recip = sem("last_recip")
        last_fnorm = sem("last_fnorm")
        last_ret = sem("last_ret")
        last_suffix = sem("last_suffix")
        last_prefix = sem("last_prefix")
        last_prefix_added = [sem(f"last_prefix_added{i}") for i in range(TU)]
        last_scale = sem("last_scale")
        last_scaled = sem("last_scaled")
        last_cumsum = sem("last_cumsum")
        last_out = sem("last_out")
        last_stored = sem("last_stored")
        warm_zero = sem("warm_zero")

        UNIT_ORDER = [[("gates", 0), ("layer0", 0), ("gates", 1), ("layer0", 1)],
                      [("gates", 2), ("layer0", 2), ("layer0", 3), ("gates", 3)]]
        FIRST_ORDER = [[("gates", 0), ("gates", 1)], UNIT_ORDER[1]]
        LAST_ORDER = [("f", 0), ("i", 0), ("f", 1), ("i", 1), ("f", 2), ("i", 2), ("c", 0), ("f", 3),
                      ("i", 3), ("c", 1), ("c", 2), ("c", 3)]
        LAST = B - 1

        block = ctx.enter_context(nc.Block())

        @block.sync
        def _(sp):
            def reload_x(b, q):
                sp.wait_ge(x1_done, KT * (b - 2) + KT)
                sp.dma_start(x_in[q][:], x_d[b]).then_inc(x_loaded[q], 16)

            def store(u, b, q, h):
                sp.wait_ge(prefix_added, 16 * (u + 1))
                sp.dma_start(out_d[b, :, TU * h:TU * h + TU, :],
                             x1[q][:, TU * h:TU * h + TU, :]).then_inc(out_stored[h], 16)

            for kt in range(KT):
                sp.dma_start(stage[0][:, kt, :], w_d[0, :, kt, :]).then_inc(w0_loaded[kt], 16)
                sp.dma_start(x_in[0][:, kt, :], x_d[0, :, kt, :]).then_inc(x0_loaded[kt], 16)
            sp.dma_start(x_in[1][:], x_d[1]).then_inc(x_loaded[1], 16)
            for m in (1, 2, 3):
                sp.dma_start(stage[m], w_d[m]).then_inc(w_loaded[m], 16)
            sp.dma_start(bias[:], bias_d).then_inc(bias_loaded, 16)
            reload_x(2, 0)
            with sp.Fori(0, 2) as j:
                for q in range(2):
                    for h in range(2):
                        store(4 * j + 2 * q + h, 2 * j + q, q, h)
                    reload_x(2 * j + 3 + q, 1 - q)
            for u in range(8, UNITS - 1):
                store(u, u // 2, u // 2 % 2, u % 2)
                if u == 9:
                    reload_x(7, 1)
            for i in range(TU):
                sp.wait_ge(last_out, i + 1)
                sp.dma_start(out_d[LAST, :, TU + i, :], x1[1][:, TU + i, :]).then_inc(last_stored, 16)
            sp.wait_ge(out_stored[0], 16 * B)
            sp.wait_ge(out_stored[1], 16 * LAST)
            sp.wait_ge(last_stored, 16 * TU)

        @block.gpsimd
        def _(pool):
            def add(addend, done, u, q, h):
                pool.dma_start(x1[q][:, TU * h:TU * h + TU, :], addend, accum_op=ALU.add)\
                    .then_inc(done, 16)

            def hidden(u, q, h):
                pool.wait_ge(cumsum_done, TU * u + TU)
                add(value[h], cumsum_added, u, q, h)
                pool.wait_ge(prefix_done, TU * u + TU)
                pool.wait_ge(cumsum_added, 16 * (u + 1))
                add(ret[h], prefix_added, u, q, h)

            pool.memset(warm[:], 0.0).then_inc(warm_zero, 1)
            for u in range(UNITS - 2):
                hidden(u, u // 2 % 2, u % 2)

            def add_last_prefix(i):
                pool.wait_ge(last_prefix, i + 1)
                pool.dma_start(x1[1][:, TU + i, :], seed[1][:, i, :], accum_op=ALU.add)\
                    .then_inc(last_prefix_added[i], 16)

            add_last_prefix(0)
            hidden(14, 1, 0)
            add_last_prefix(1)

        @block.tensor
        def _(pe):
            def product(ps, m, ht, kt, x_hi, x_lo):
                cols = slice(ht * P, ht * P + P)
                pe.matmul(ps[:], w_hi[m][:, kt, cols], x_hi[:, kt, :], start=kt == 0, stop=False)
                pe.matmul(ps[:], w_lo[m][:, kt, cols], x_hi[:, kt, :], start=False, stop=False)
                return pe.matmul(ps[:], w_hi[m][:, kt, cols], x_lo[:, kt, :], start=False,
                                 stop=kt == KT - 1)

            def layer0(b, q, ht, ps=None):
                n = KT * b + ht
                if ps is None:
                    ps = layer0_ps[ht % 2]
                    pe.wait_ge(x1_done, n - 1)
                for kt in range(KT):
                    if ht == 0:
                        pe.wait_ge(xs_lo_done, KT * b + kt + 1)
                    last = product(ps, 0, ht, kt, xs_hi[q], xs_lo[q])
                last.then_inc(layer0_mm, 1)

            def gate(g, b, q, ht, ps):
                for kt in range(KT):
                    if ht == 0 and g == 0:
                        pe.wait_ge(x1_lo_done, KT * b + kt + 1)
                    last = product(ps, 1 + g, ht, kt, x1_hi[q], x1_lo[q])
                last.then_inc(gate_mm[g], 1)

            def bank_read(g, n):
                pe.wait_ge((sig_f_done, sig_i_done, cand_done)[g], n - 1)

            def gates(b, q, ht, first):
                for g in range(GATES):
                    if first and ht == 0:
                        pe.wait_ge(w_lo_done, 1 + g)
                    if first and ht < 2:
                        if (g, ht) != (0, 0):
                            pe.wait_ge(x1_done, {(1, 0): 3, (2, 0): 3, (0, 1): 5, (1, 1): 6, (2, 1): 6}[g, ht])
                    else:
                        bank_read(g, KT * b + ht)
                    gate(g, b, q, ht, gate_ps[g][ht % 2])

            def phase(b, q, order=UNIT_ORDER, first=False):
                for h in range(2):
                    for what, ht in order[h]:
                        if what == "gates":
                            gates(b, q, ht, first)
                        else:
                            layer0(b + 1, 1 - q, ht)

            pe.wait_ge(warm_zero, 1)
            for _ in range(WARM):
                pe.matmul(demod_ps[:], warm[:, 0:P], warm[:], start=True, stop=True)
            for kt in range(KT):
                pe.wait_ge(w0_lo_done, kt + 1)
                pe.wait_ge(xs_lo_done, kt + 1)
                for ht in range(KT):
                    last = product(early_ps[0, ht], 0, ht, kt, xs_hi[0], xs_lo[0])
                    if kt == KT - 1:
                        last.then_inc(layer0_mm, 1)
            pe.wait_ge(ys_done, 4)
            pe.wait_ge(w0_sq_lo_done, 1)
            for ht in range(KT):
                cols = slice(ht * P, ht * P + P)
                c = 2 * B * ht
                for kt in range(KT):
                    pe.matmul(demod_ps[:, c:c + 2 * B], w0_sq_hi[:, kt, cols],
                              ys_sq_parts[:, kt].rearrange("p a b -> p (a b)"), start=kt == 0, stop=False)
                    last = pe.matmul(demod_ps[:, c:c + B], w0_sq_lo[:, kt, cols],
                                     ys_sq_parts[:, kt, 0, :], start=False, stop=kt == KT - 1)
            last.then_inc(demod_mm, 1)
            for ht in range(2):
                layer0(1, 1, ht, early_ps[1, ht])
            phase(0, 0, FIRST_ORDER, first=True)
            with pe.Fori(0, 3) as j:
                phase(2 * j + 1, 1)
                phase(2 * j + 2, 0)
            for what, ht in LAST_ORDER:
                g = "fic".index(what)
                if g < 2 or ht < 2:
                    bank_read(g, KT * LAST + ht)
                gate(g, LAST, LAST % 2, ht, late_cand_ps[ht] if g == 2 else gate_ps[g][ht % 2])

        @block.scalar
        def _(act):
            def split_x_tile(b, q, kt):
                act.activation(xs_hi[q][:, kt, :], x_in[q][:, kt, :], ACT.Copy,
                               scale=ys[:, kt, bass.ds(b, 1)]).then_inc(xs_hi_done, 1)

            def split_x1(b, q, ht):
                act.wait_ge(x1_done, KT * b + ht + 1)
                act.activation(x1_hi[q][:, ht, :], x1[q][:, ht, :], ACT.Copy).then_inc(x1_hi_done, 1)

            def split_w(m):
                act.wait_ge(w_loaded[m], 16)
                act.activation(w_hi[m][:], stage[m], ACT.Copy).then_inc(w_hi_done, 1)

            def sigmoids(b, ht, v):
                n = KT * b + ht
                for g, (dst, done) in enumerate(((forget[v], sig_f_done), (value[v], sig_i_done))):
                    act.wait_ge(gate_mm[g], n + 1)
                    act.activation(dst[:, ht % TU, :], gate_ps[g][ht % 2][:], ACT.Sigmoid,
                                   bias=bias[:, g, ht:ht + 1]).then_inc(done, 1)

            def recip_seed(u, v):
                act.preload_act_table_set(LN_EXP_SET)
                act.wait_ge(gsum_done, TU * u + TU)
                act.activation(seed[v], gsum[v], ACT.Ln).then_inc(ln_done, 1)
                act.wait_ge(ln_done, u + 1)
                act.activation(seed[v], seed[v], ACT.Exp, scale=-1.0).then_inc(seed_done, 1)
                act.preload_act_table_set(SIGMOID_SET)

            def retention(u, v):
                act.wait_ge(fnorm_done, u + 1)
                act.activation(ret[v], forget[v], ACT.Copy, bias=GATE_EPS).then_inc(ret_done, 1)

            def step(u, b, q, h, split=None, order=UNIT_ORDER, free=True):
                v = 1 - h
                if split is not None:
                    sb, sq, loads = split
                    act.wait_ge(x_loaded[sq], 16 * loads)
                    act.wait_ge(layer0_mm, KT * (sb - 2) + KT)
                    for kt in range(KT):
                        split_x_tile(sb, sq, kt)
                recip_seed(u, v)
                if free:
                    act.wait_ge(cumsum_added, 16 * u)
                for k, (what, ht) in enumerate(order[h]):
                    if k == 1 and free:
                        act.wait_ge(prefix_added, 16 * u)
                    if what == "gates":
                        sigmoids(b, ht, h)
                    else:
                        split_x1(b + 1, 1 - q, ht)
                    if k == 0:
                        retention(u, v)

            act.dma_start(y[:], y_d).then_inc(y_loaded, 16)
            act.preload_act_table_set("sqrt_and_others")
            for kt in range(KT):
                act.wait_ge(w0_loaded[kt], 16)
                act.activation(w_hi[0][:, kt, :], stage[0][:, kt, :], ACT.Copy).then_inc(w0_hi_done, 1)
                if kt == 0:
                    act.wait_ge(ys_done, 1)
                act.wait_ge(x0_loaded[kt], 16)
                split_x_tile(0, 0, kt)
            act.activation(w0_sq[:], stage[0], ACT.Square).then_inc(w0_sq_done, 1)
            act.wait_ge(w0_sq_done, 1)
            act.activation(w0_sq_hi[:], w0_sq[:], ACT.Copy).then_inc(w0_sq_done, 1)
            act.wait_ge(x_loaded[1], 16)
            for kt in range(KT):
                split_x_tile(1, 1, kt)
            split_w(1)
            split_w(2)
            act.wait_ge(demod_step, 2)
            act.activation(demod_root[:], demod_sum[:], ACT.Sqrt).then_inc(root_done, 1)
            for ht in range(KT):
                split_x1(0, 0, ht)
            split_w(3)
            for ht in range(2):
                split_x1(1, 1, ht)
            act.preload_act_table_set(SIGMOID_SET)
            act.wait_ge(bias_loaded, 16)
            for ht in range(2):
                sigmoids(0, ht, 0)
            step(0, 0, 0, 1, free=False)
            with act.Fori(0, 3) as j:
                for k in range(1, 5):
                    front = k + 1
                    q = (k - 1) // 2
                    split = (2 * j + q + 2, q, j + 1 + q) if k % 2 else None
                    step(4 * j + k, 2 * j + front // 2, front // 2 % 2, front % 2, split)
            step(13, LAST, 1, 0, order=[[("gates", 0), ("gates", 1)]])
            recip_seed(14, 0)
            act.wait_ge(cumsum_added, 16 * 14)
            sigmoids(LAST, 2, 1)
            retention(14, 0)
            act.preload_act_table_set(LN_EXP_SET)
            for i in range(TU):
                act.wait_ge(gsum_done, KT * LAST + TU + i + 1)
                act.activation(seed[1][:, i, :], gsum[1][:, i, :], ACT.Ln).then_inc(last_seed, 1)
                act.wait_ge(last_seed, 2 * i + 1)
                act.activation(seed[1][:, i, :], seed[1][:, i, :], ACT.Exp, scale=-1.0)\
                    .then_inc(last_seed, 1)
                if i == 0:
                    act.preload_act_table_set(SIGMOID_SET)
                    sigmoids(LAST, 3, 1)
                    act.preload_act_table_set(LN_EXP_SET)
                    act.wait_ge(prefix_added, 16 * 14)
                act.wait_ge(last_fnorm, i + 1)
                act.activation(ret[1][:, i, :], forget[1][:, i, :], ACT.Copy, bias=GATE_EPS)\
                    .then_inc(last_ret, 1)

        @block.vector
        def _(dve):
            def split_x_tile(b, q, kt):
                dve.wait_ge(xs_hi_done, KT * b + kt + 1)
                dve.scalar_tensor_tensor(xs_lo[q][:, kt, :], x_in[q][:, kt, :],
                                         ys[:, kt, bass.ds(b, 1)], xs_hi[q][:, kt, :].bitcast(F32),
                                         ALU.mult, ALU.subtract).then_inc(xs_lo_done, 1)

            def split_w(m):
                dve.wait_ge(w_hi_done, m)
                dve.tensor_tensor(w_lo[m][:], stage[m], w_hi[m][:].bitcast(F32), ALU.subtract)\
                    .then_inc(w_lo_done, 1)

            def residual0(b, q, ht, ps=None):
                dve.wait_ge(layer0_mm, KT * b + ht + 1)
                dve.scalar_tensor_tensor(x1[q][:, ht, :], (ps or layer0_ps[ht % 2])[:],
                                         demod[:, ht, bass.ds(b, 1)], x_in[q][:, ht, :],
                                         ALU.mult, ALU.add).then_inc(x1_done, 1)

            def split_x1(b, q, ht):
                dve.wait_ge(x1_hi_done, KT * b + ht + 1)
                dve.tensor_tensor(x1_lo[q][:, ht, :], x1[q][:, ht, :], x1_hi[q][:, ht, :].bitcast(F32),
                                  ALU.subtract).then_inc(x1_lo_done, 1)

            def gate_sum(b, ht, v):
                t = ht % TU
                dve.wait_ge(sig_i_done, KT * b + ht + 1)
                dve.scalar_tensor_tensor(gsum[v][:, t, :], forget[v][:, t, :], GATE_EPS,
                                         value[v][:, t, :], ALU.add, ALU.add).then_inc(gsum_done, 1)

            def candidate(b, ht, v, ps):
                t = ht % TU
                dve.wait_ge(gate_mm[2], KT * b + ht + 1)
                dve.wait_ge(gsum_done, KT * b + ht + 1)
                dve.scalar_tensor_tensor(value[v][:, t, :], ps[:], bias[:, 2, ht:ht + 1],
                                         value[v][:, t, :], ALU.add, ALU.mult).then_inc(cand_done, 1)

            def norms(u, v):
                dve.wait_ge(seed_done, u + 1)
                dve.scalar_tensor_tensor(gsum[v], gsum[v], -1.0, seed[v], ALU.mult, ALU.mult)\
                    .then_inc(newton_done, 1)
                dve.wait_ge(newton_done, u + 1)
                dve.scalar_tensor_tensor(gsum[v], gsum[v], 2.0, seed[v], ALU.add, ALU.mult)\
                    .then_inc(recip_done, 1)
                dve.wait_ge(recip_done, u + 1)
                dve.tensor_tensor(forget[v], forget[v], gsum[v], ALU.mult).then_inc(fnorm_done, 1)

            def new_info(u, v):
                dve.wait_ge(cand_done, TU * u + TU)
                dve.tensor_tensor(value[v], value[v], gsum[v], ALU.mult).then_inc(info_done, 1)

            def suffix_products(u, v):
                dve.wait_ge(ret_done, u + 1)
                for t in range(TU):
                    dve.tensor_tensor_scan(forget[v][:, t, ::-1], ret[v][:, t, ::-1],
                                           ret[v][:, t, ::-1], 1.0, ALU.mult, ALU.bypass)\
                        .then_inc(suffix_done, 1)

            def scaled_info(u, v):
                dve.wait_ge(info_done, u + 1)
                dve.wait_ge(suffix_done, TU * u + TU)
                dve.tensor_tensor(value[v], value[v], forget[v], ALU.mult).then_inc(scaled_done, 1)

            def prefix_products(u, v, b):
                dve.wait_ge(suffix_done, TU * u + TU)
                for t in range(TU):
                    dve.tensor_tensor_scan(ret[v][:, t, :], ret[v][:, t, :], ret[v][:, t, :],
                                           y[:, TU * v + t, bass.ds(b, 1)], ALU.mult, ALU.bypass)\
                        .then_inc(prefix_done, 1)

            def cumsum(v, t, done):
                dve.tensor_tensor_scan(value[v][:, t, :], value[v][:, t, :], value[v][:, t, :], 0.0,
                                       ALU.add, ALU.bypass).then_inc(done, 1)

            def step(u, b, q, h, bu, split=None, stored=None, order=UNIT_ORDER):
                v = 1 - h
                if split is not None:
                    for kt in range(KT):
                        split_x_tile(*split, kt)
                norms(u, v)
                new_info(u, v)

                def gate_tile(ht):
                    gate_sum(b, ht, h)
                    if b is not LAST:
                        candidate(b, ht, h, gate_ps[2][ht % 2])

                front = order[h]
                gate_tile(front[0][1])
                suffix_products(u, v)
                if b is not LAST:
                    if stored is not None:
                        dve.wait_ge(out_stored[h], 16 * stored)
                    residual0(b + 1, 1 - q, front[1][1])
                scaled_info(u, v)
                if b is not LAST:
                    split_x1(b + 1, 1 - q, front[1][1])
                if b is LAST:
                    gate_tile(front[1][1])
                dve.wait_ge(scaled_done, u + 1)
                for t in range(TU):
                    cumsum(v, t, cumsum_done)
                prefix_products(u, v, bu)
                if front[2:3] == [("layer0", 3)]:
                    residual0(b + 1, 1 - q, 3)
                for what, ht in front[2:]:
                    if what == "gates":
                        gate_tile(ht)
                    else:
                        if ht != 3:
                            residual0(b + 1, 1 - q, ht)
                        split_x1(b + 1, 1 - q, ht)

            dve.wait_ge(y_loaded, 16)
            dve.tensor_scalar(ys[:], y[:], Y_SCALE, None, ALU.mult).then_inc(ys_done, 1)
            dve.wait_ge(ys_done, 1)
            dve.tensor_tensor(ys_sq[:], ys[:], ys[:], ALU.mult).then_inc(ys_done, 1)
            dve.wait_ge(ys_done, 2)
            dve.tensor_copy(ys_sq_parts[:, :, 0, :], ys_sq[:]).then_inc(ys_done, 1)
            dve.wait_ge(ys_done, 3)
            dve.tensor_tensor(ys_sq_parts[:, :, 1, :], ys_sq[:], ys_sq_parts[:, :, 0, :].bitcast(F32),
                              ALU.subtract).then_inc(ys_done, 1)
            for kt in range(KT):
                dve.wait_ge(w0_hi_done, kt + 1)
                dve.tensor_tensor(w_lo[0][:, kt, :], stage[0][:, kt, :], w_hi[0][:, kt, :].bitcast(F32),
                                  ALU.subtract).then_inc(w0_lo_done, 1)
                split_x_tile(0, 0, kt)
            dve.wait_ge(w0_sq_done, 2)
            dve.tensor_tensor(w0_sq_lo[:], w0_sq[:], w0_sq_hi[:].bitcast(F32), ALU.subtract)\
                .then_inc(w0_sq_lo_done, 1)
            for kt in range(KT):
                split_x_tile(1, 1, kt)
            split_w(1)
            split_w(2)
            sums = demod_ps[:, 0:2 * B * KT].rearrange("p (k a b) -> p k a b", a=2, b=B)
            total, root, inverse, d = demod_sum[:], demod_root[:], demod_seed[:], demod[:]
            dve.wait_ge(demod_mm, 1)
            dve.tensor_scalar(total, sums[:, :, 0, :], LAYER_EPS, None, ALU.add).then_inc(demod_step, 1)
            dve.wait_ge(demod_step, 1)
            dve.tensor_tensor(total, sums[:, :, 1, :], total, ALU.add).then_inc(demod_step, 1)
            dve.wait_ge(root_done, 1)
            dve.reciprocal(inverse, root).then_inc(demod_step, 1)
            dve.wait_ge(demod_step, 3)
            dve.tensor_tensor(d, total, inverse, ALU.mult).then_inc(demod_step, 1)
            dve.wait_ge(demod_step, 4)
            dve.tensor_tensor(d, d, inverse, ALU.mult).then_inc(demod_step, 1)
            dve.wait_ge(demod_step, 5)
            dve.tensor_scalar(d, d, -0.5, 1.5, ALU.mult, ALU.add).then_inc(demod_step, 1)
            dve.wait_ge(demod_step, 6)
            dve.tensor_tensor(d, d, inverse, ALU.mult).then_inc(demod_step, 1)
            dve.wait_ge(demod_step, 7)
            for ht in range(KT):
                residual0(0, 0, ht, early_ps[0, ht])
                if ht:
                    split_x1(0, 0, ht - 1)
            split_x1(0, 0, KT - 1)
            for ht in range(2):
                residual0(1, 1, ht, early_ps[1, ht])
            split_w(3)
            for ht in range(2):
                split_x1(1, 1, ht)
            dve.wait_ge(bias_loaded, 16)
            for ht in range(2):
                gate_sum(0, ht, 0)
                candidate(0, ht, 0, gate_ps[2][ht % 2])
            step(0, 0, 0, 1, 0, order=FIRST_ORDER)
            with dve.Fori(0, 3) as j:
                for k in range(1, 5):
                    front = k + 1
                    split = (2 * j + (k - 1) // 2 + 2, (k - 1) // 2) if k % 2 else None
                    step(4 * j + k, 2 * j + front // 2, front // 2 % 2, front % 2, 2 * j + k // 2,
                         split, 2 * j + (k - 1) // 2 + 1)
            step(13, LAST, 1, 0, LAST - 1, order=[[("gates", 0), ("gates", 1)]])

            def last_candidate(ht):
                candidate(LAST, ht, ht // TU, late_cand_ps[ht])

            def last_norms(i):
                g, s, f = gsum[1][:, i, :], seed[1][:, i, :], forget[1][:, i, :]
                dve.wait_ge(last_seed, 2 * i + 2)
                dve.scalar_tensor_tensor(g, g, -1.0, s, ALU.mult, ALU.mult).then_inc(last_recip, 1)
                dve.wait_ge(last_recip, 2 * i + 1)
                dve.scalar_tensor_tensor(g, g, 2.0, s, ALU.add, ALU.mult).then_inc(last_recip, 1)
                dve.wait_ge(last_recip, 2 * i + 2)
                dve.tensor_tensor(f, f, g, ALU.mult).then_inc(last_fnorm, 1)

            def last_scans(i):
                r, f, g = ret[1][:, i, :], forget[1][:, i, :], gsum[1][:, i, :]
                dve.wait_ge(last_ret, i + 1)
                dve.tensor_tensor_scan(seed[1][:, i, :], r, r, y[:, TU + i, LAST:LAST + 1], ALU.mult,
                                       ALU.bypass).then_inc(last_prefix, 1)
                dve.tensor_tensor_scan(f[:, ::-1], r[:, ::-1], r[:, ::-1], 1.0, ALU.mult, ALU.bypass)\
                    .then_inc(last_suffix, 1)
                dve.wait_ge(last_suffix, i + 1)
                dve.tensor_tensor(g, g, f, ALU.mult).then_inc(last_scale, 1)

            def last_output(i):
                val, out = value[1][:, i, :], x1[1][:, TU + i, :]
                dve.wait_ge(cand_done, KT * LAST + TU + i + 1)
                dve.wait_ge(last_scale, i + 2)
                dve.tensor_tensor(val, val, gsum[1][:, i, :], ALU.mult).then_inc(last_scaled, 1)
                dve.wait_ge(last_scaled, i + 1)
                cumsum(1, i, last_cumsum)
                dve.wait_ge(last_cumsum, i + 1)
                dve.wait_ge(last_prefix_added[i], 16)
                dve.tensor_tensor(out, out, val, ALU.add).then_inc(last_out, 1)

            norms(14, 0)
            gate_sum(LAST, 2, 1)
            last_candidate(0)
            suffix_products(14, 0)
            prefix_products(14, 0, LAST)
            dve.tensor_tensor(gsum[0], gsum[0], forget[0], ALU.mult).then_inc(last_scale, 1)
            last_norms(0)
            gate_sum(LAST, 3, 1)
            last_scans(0)
            last_candidate(1)
            dve.wait_ge(last_scale, 1)
            dve.wait_ge(cand_done, KT * LAST + TU)
            dve.tensor_tensor(value[0], value[0], gsum[0], ALU.mult).then_inc(scaled_done, 1)
            dve.wait_ge(scaled_done, 15)
            for t in range(TU):
                cumsum(0, t, cumsum_done)
            last_candidate(2)
            last_norms(1)
            last_output(0)
            last_scans(1)
            last_candidate(3)
            last_output(1)


def kernel(x, cond_1024, L0_cond_weight, L1_cond_W_f, L1_cond_b_f, L1_cond_W_i, L1_cond_b_i,
           L1_cond_W_h, L1_cond_b_h):
    import concourse.bacc as bacc
    from concourse.bass_utils import run_bass_kernel_spmd

    def tiled(a):
        return np.asarray(a).reshape(KT, P, -1).transpose(1, 0, 2)

    arrays = {
        "x": np.ascontiguousarray(np.asarray(x).reshape(B, S, KT, P).transpose(0, 3, 2, 1)),
        "y": np.ascontiguousarray(tiled(np.asarray(cond_1024).T)),
        "bias": np.ascontiguousarray(np.stack(
            [np.asarray(v).reshape(KT, P).T for v in (L1_cond_b_f, L1_cond_b_i, L1_cond_b_h)], axis=1)),
        "w": np.ascontiguousarray(np.stack(
            [tiled(L0_cond_weight)] + [tiled(np.asarray(w).T) for w in (L1_cond_W_f, L1_cond_W_i, L1_cond_W_h)])),
    }
    nc = bacc.Bacc("TRN2", target_bir_lowering=False, num_devices=1)
    aps = {n: nc.dram_tensor("in_" + n, a.shape, F32, kind="ExternalInput").ap() for n, a in arrays.items()}
    out = nc.dram_tensor("out", (B, P, KT, S), F32, kind="ExternalOutput").ap()
    build(nc, aps["x"], aps["y"], aps["bias"], aps["w"], out)
    r = run_bass_kernel_spmd(nc, [{"in_" + n: a for n, a in arrays.items()}], core_ids=[0])
    return np.ascontiguousarray(r.results[0]["out"].transpose(0, 3, 2, 1)).reshape(B, S, D)
```
